# Optimizing a Trainium2 kernel written in Bass

```python
import numpy as np
import jax
import jax.numpy as jnp

def _softmax(x, axis=-1):
    return jax.nn.softmax(x, axis=axis)

def _gelu(x):
    return jax.nn.gelu(x, approximate=True)

def _silu(x):
    return jax.nn.silu(x)

def _sigmoid(x):
    return jax.nn.sigmoid(x)

def _layernorm(x, axis=-1, eps=1e-05):
    m = jnp.mean(x, axis=axis, keepdims=True)
    v = jnp.var(x, axis=axis, keepdims=True)
    return (x - m) / jnp.sqrt(v + eps)

def _scatter_add(tgt, idx, src, axis=0):
    return tgt.at[idx].add(src)

def _segment_sum(src, seg, n):
    return jax.ops.segment_sum(src, seg, n)
kernel_name = 'mk_cond_seq_d1_seqx_r4_1c38c2'

def setup_inputs(seed: int=0):
    np.random.seed(seed)
    _w = jnp.asarray

    def _rec_inputs():
        import jax
        import jax.numpy as jnp
        _rk = jax.random.key(seed)
        x = -0.0003929 + 0.9999 * jax.random.normal(jax.random.fold_in(_rk, 1), (8, 256, 256), jnp.float32)
        _lenS = 256 - jax.random.randint(jax.random.fold_in(_rk, 7), (8,), 0, max(1, 256 // 4) + 1, jnp.int32)
        _lenS2 = 256 - jax.random.randint(jax.random.fold_in(_rk, 8), (8,), 0, max(1, 256 // 4) + 1, jnp.int32)
        cond_1024 = 0.0061147 + 1.02565 * jax.random.normal(jax.random.fold_in(_rk, 11), (8, 256), jnp.float32)
        return (x, cond_1024)
    x, cond_1024 = _rec_inputs()

    def _L0_cond_setup():
        import jax, jax.numpy as jnp
        import numpy as np
        H = 16
        EPS = 1e-05

        def layer_norm(x, g, b):
            mu = jnp.mean(x, axis=-1, keepdims=True)
            var = jnp.var(x, axis=-1, keepdims=True)
            return (x - mu) * jax.lax.rsqrt(var + EPS) * g + b
        key = jax.random.key(seed)
        ks = jax.random.split(key, 8)
        B, T, D, TE = (4, 1024, 256, 256)
        s = 0.02
        return {'x': jax.random.normal(ks[0], (B, T, D), jnp.float32), 'emb': jax.random.normal(ks[1], (B, 1, TE), jnp.float32), 'gate_msa': jax.random.normal(ks[2], (B, 1, D), jnp.float32), 'norm_g': jnp.ones((D,), jnp.float32), 'norm_b': jnp.zeros((D,), jnp.float32), 'Wq': jax.random.normal(ks[3], (D, D), jnp.float32) * s, 'bq': jnp.zeros((D,), jnp.float32), 'Wk': jax.random.normal(ks[4], (D, D), jnp.float32) * s, 'bk': jnp.zeros((D,), jnp.float32), 'Wv': jax.random.normal(ks[5], (D, D), jnp.float32) * s, 'bv': jnp.zeros((D,), jnp.float32), 'emb_W': jax.random.normal(ks[6], (TE, 2 * D), jnp.float32) * s, 'emb_b': jnp.zeros((2 * D,), jnp.float32), 'sn_g': jnp.ones((D,), jnp.float32), 'sn_b': jnp.zeros((D,), jnp.float32), 'out_W': jax.random.normal(ks[7], (D, D), jnp.float32) * s, 'out_b': jnp.zeros((D,), jnp.float32)}
    _L0_cond_all = _L0_cond_setup()
    _L0_cond_in = {k: v for k, v in _L0_cond_all.items() if k in ('norm_g', 'norm_b', 'Wq', 'bq', 'Wk', 'bk', 'Wv', 'bv', 'emb_W', 'emb_b', 'sn_g', 'sn_b', 'out_W', 'out_b')}
    del _L0_cond_all
    return {'x': x, 'cond_1024': cond_1024, 'L0_cond_norm_g': _L0_cond_in['norm_g'], 'L0_cond_norm_b': _L0_cond_in['norm_b'], 'L0_cond_Wq': _L0_cond_in['Wq'], 'L0_cond_bq': _L0_cond_in['bq'], 'L0_cond_Wk': _L0_cond_in['Wk'], 'L0_cond_bk': _L0_cond_in['bk'], 'L0_cond_Wv': _L0_cond_in['Wv'], 'L0_cond_bv': _L0_cond_in['bv'], 'L0_cond_emb_W': _L0_cond_in['emb_W'], 'L0_cond_emb_b': _L0_cond_in['emb_b'], 'L0_cond_sn_g': _L0_cond_in['sn_g'], 'L0_cond_sn_b': _L0_cond_in['sn_b'], 'L0_cond_out_W': _L0_cond_in['out_W'], 'L0_cond_out_b': _L0_cond_in['out_b']}

def reference(x, cond_1024, L0_cond_norm_g, L0_cond_norm_b, L0_cond_Wq, L0_cond_bq, L0_cond_Wk, L0_cond_bk, L0_cond_Wv, L0_cond_bv, L0_cond_emb_W, L0_cond_emb_b, L0_cond_sn_g, L0_cond_sn_b, L0_cond_out_W, L0_cond_out_b):
    import jax
    import jax.numpy as jnp

    def _L0_cond_ref(x, emb, gate_msa, norm_g, norm_b, Wq, bq, Wk, bk, Wv, bv, emb_W, emb_b, sn_g, sn_b, out_W, out_b):
        import jax, jax.numpy as jnp
        import numpy as np
        H = 16
        EPS = 1e-05

        def layer_norm(x, g, b):
            mu = jnp.mean(x, axis=-1, keepdims=True)
            var = jnp.var(x, axis=-1, keepdims=True)
            return (x - mu) * jax.lax.rsqrt(var + EPS) * g + b
        B, T, D = x.shape
        dh = D // H
        xn = layer_norm(x, norm_g, norm_b)
        q = (xn @ Wq + bq).reshape(B, T, H, dh)
        k = (xn @ Wk + bk).reshape(B, T, H, dh)
        v = (xn @ Wv + bv).reshape(B, T, H, dh)
        q = jax.nn.softmax(q, axis=-1)
        k = jax.nn.softmax(k, axis=1)
        ctx = jnp.einsum('bnhd,bnhl->bhdl', k, v)
        y = jnp.einsum('bnhd,bhdl->bnhl', q, ctx).reshape(B, T, D)
        emb_out = jax.nn.silu(emb) @ emb_W + emb_b
        scale, shift = jnp.split(emb_out, 2, axis=-1)
        h = layer_norm(y, sn_g, sn_b) * (1.0 + scale) + shift
        h = jax.nn.silu(h) @ out_W + out_b
        return x + gate_msa * h
    x = _L0_cond_ref(x, cond_1024[:, None, :], cond_1024[:, None, :], L0_cond_norm_g, L0_cond_norm_b, L0_cond_Wq, L0_cond_bq, L0_cond_Wk, L0_cond_bk, L0_cond_Wv, L0_cond_bv, L0_cond_emb_W, L0_cond_emb_b, L0_cond_sn_g, L0_cond_sn_b, L0_cond_out_W, L0_cond_out_b)
    return x

_drawn_inputs = setup_inputs


def setup_inputs(seed=0):
    import zlib

    import numpy as np

    out = dict(_drawn_inputs(seed))
    spreads = {'L0_cond_norm_g': (1.0, 0.6),
     'L0_cond_norm_b': (0.0, 0.315),
     'L0_cond_bq': (0.0, 0.8),
     'L0_cond_bk': (0.0, 2.0),
     'L0_cond_bv': (0.0, 0.1),
     'L0_cond_emb_b': (0.0, 0.1),
     'L0_cond_sn_g': (1.0, 0.2),
     'L0_cond_sn_b': (0.0, 0.407),
     'L0_cond_out_b': (0.0, 0.1)}
    factors = {'L0_cond_Wq': 8.0, 'L0_cond_Wk': 8.0}
    for name, (base, spread) in spreads.items():
        noise = np.random.default_rng([zlib.crc32(name.encode()), seed]).standard_normal(out[name].shape)
        drawn = base * np.exp(spread * noise) if base else spread * noise
        out[name] = jnp.asarray(drawn.astype(out[name].dtype))
    for name, factor in factors.items():
        out[name] = (out[name] * factor).astype(out[name].dtype)
    return out
```

```python
from contextlib import ExitStack

import numpy as np

import concourse.bass as bass
from concourse import mybir

F32 = mybir.dt.float32
F32R = mybir.dt.float32r
ALU = mybir.AluOpType
ACT = mybir.ActivationFunctionType
AX = mybir.AxisListType

P = 128
HEADS = 16
EPS = 1e-5


def linear_attention_block(nc, x, cond, norm_g, norm_b, wq, bq, wk, bk, wv, bv,
                           emb_w, emb_b, sn_g, sn_b, out_w, out_b, out):
    B, N, D = x.shape
    T, C = N // P, D // P
    DH = D // HEADS
    HC = P // DH
    W = DH + 1
    assert T == 2 and C == 2 and B % 2 == 0 and B >= 4

    ctx = ExitStack()
    with ctx:
        def sb(name, shape, dt=F32):
            return ctx.enter_context(nc.sbuf_tensor(name, shape, dt))

        def psum(name, shape):
            return ctx.enter_context(nc.psum_tensor(name, shape, F32))

        def sem(name):
            return ctx.enter_context(nc.semaphore(name))

        w_raw = {n: sb(f"w{n}_raw", [P, C, D]) for n in "qkvo"}
        w_hi = {n: sb(f"w{n}_hi", [P, C, D], F32R) for n in "qkvo"}
        w_lo = {n: sb(f"w{n}_lo", [P, C, D], F32R) for n in "qkvo"}
        emb_sb = sb("emb_sb", [P, C, 2 * D])
        NV = 2 * B + 14
        vec_rows = sb("vec_rows", [NV, P])
        vec = sb("vec", [P, NV])
        at = 2 * B
        cond_v = vec[:, 0:at].rearrange("p (b c) -> p c b", c=C)
        g_v, b_v, bk_v, sng_v, snb_v = (vec[:, at + 2 * k:at + 2 * k + 2] for k in range(5))
        embb_v = vec[:, at + 10:at + 14]
        bqv_row = sb("bqv_row", [1, 2, D])
        outb_bc = sb("outb_bc", [P, D])
        gate_bc = sb("gate_bc", [P, B, D])
        ident = sb("ident", [P, P])
        ones = sb("ones", [P, P])
        head_mask = sb("head_mask", [P, HC, W])
        minus_half = sb("minus_half", [P, 2])
        bias_sel = sb("bias_sel", [P, P], F32R)
        bias_self = sb("bias_self", [P, P])
        bq_rows = sb("bq_rows", [P, D], F32R)
        cqv_sb = sb("cqv_sb", [P, 2, D])
        ck_sb = sb("ck_sb", [P, C])
        cv_blk = sb("cv_blk", [P, C, HC, DH])
        silu_e = sb("silu_e", [P, C, B])
        silu_1e = sb("silu_1e", [P, C, B])
        silu_r = sb("silu_r", [P, C, B])
        silu_c = sb("silu_c", [P, C, B])
        emb_o = sb("emb_o", [P, 2 * C, B])
        scale1 = sb("scale1", [P, C, B])
        shift_t = sb("shift_t", [P, C, B])
        h_scale = sb("h_scale", [P, B, C])
        h_bias = sb("h_bias", [P, B, C])

        x_all = sb("x_all", [P, B, T, D])
        h_all = sb("h_all", [P, B, C, N])
        st1 = sb("st1", [P, T, 6])
        mv1 = sb("mv1", [P, T, 2])
        ve1 = sb("ve1", [P, T])
        rstd1 = sb("rstd1", [P, T])
        xhat = sb("xhat", [P, T, D])
        xt_hi = sb("xt_hi", [P, 2, C, N], F32R)
        xt_lo = sb("xt_lo", [P, 2, C, N], F32R)
        kmax0 = sb("kmax0", [P, C])
        kmax = sb("kmax", [P, C])
        kbias = sb("kbias", [P, C])
        ksum = sb("ksum", [P, C])
        krec = sb("krec", [P, C])
        ek = sb("ek", [P, C, N])
        ek_tok = sb("ek_tok", [P, T, D])
        qmax = sb("qmax", [P, T, HEADS])
        q_sh = sb("q_sh", [P, T, D])
        eq = sb("eq", [P, C, N])
        v_tok = sb("v_tok", [P, T, D])
        ctx_m = sb("ctx_m", [P, C, HC, DH])
        ctx_bd = sb("ctx_bd", [P, C, HC, W])
        qrec = sb("qrec", [P, T, HEADS])
        y = sb("y", [P, T, D])
        st2 = sb("st2", [P, T, 6])
        mv2 = sb("mv2", [P, T, 2])
        ve2 = sb("ve2", [P, T])
        rstd2 = sb("rstd2", [P, T])
        yhat = sb("yhat", [P, T, D])
        gob = sb("gob", [P, D])
        s_f = sb("s_f", [P, 2, C, N])
        s_hi = sb("s_hi", [P, 2, C, N], F32R)
        s_lo = sb("s_lo", [P, 2, C, N], F32R)
        o_g = sb("o_g", [P, 2, T, D])

        ps_x = psum("ps_x", [P, C, N])
        ps_k = psum("ps_k", [P, C, N])
        ps_q = psum("ps_q", [P, T, D])
        ps_v = psum("ps_v", [P, T, D])
        ps_ek = psum("ps_ek", [P, T, D])
        ps_c = psum("ps_c", [P, C, 2 * P])
        ps_y = psum("ps_y", [P, 2, 512])

        x0_in, x1_in, xr_in = sem("x0_in"), sem("x1_in"), sem("xr_in")
        w_in = {n: sem(f"w{n}_in") for n in "qkvo"}
        vec_in, row_in, gate_in, emb_in = sem("vec_in"), sem("row_in"), sem("gate_in"), sem("emb_in")
        blank_done = sem("blank_done")
        ident_done, mask_done, const_done = sem("ident_done"), sem("mask_done"), sem("const_done")
        vec_t_done, vec_done = sem("vec_t_done"), sem("vec_done")
        w_hi_done, w_lo_done = sem("w_hi_done"), sem("w_lo_done")
        ck_mm_done, cqv_mm_done, emb_mm_done = sem("ck_mm_done"), sem("cqv_mm_done"), sem("emb_mm_done")
        ck_done, cqv_done, bq_rows_done = sem("ck_done"), sem("cqv_done"), sem("bq_rows_done")
        cv_done, silu_e_done, silu_c_done = sem("cv_done"), sem("silu_e_done"), sem("silu_c_done")
        small_done, affine_done = sem("small_done"), sem("affine_done")
        xt_mm, k_mm, q_mm, v_mm = sem("xt_mm"), sem("k_mm"), sem("q_mm"), sem("v_mm")
        ekt_mm, qt_mm, ctx_mm, y_mm, yt_mm = (sem(n) for n in ("ekt_mm", "qt_mm", "ctx_mm", "y_mm", "yt_mm"))
        st1_done, mv1_done = sem("st1_done"), sem("mv1_done")
        ve1_done, rstd1_done, xhat_done = sem("ve1_done"), sem("rstd1_done"), sem("xhat_done")
        xt_hi_done, xt_lo_done = sem("xt_hi_done"), sem("xt_lo_done")
        kmax0_done, kmax_done, kbias_done = sem("kmax0_done"), sem("kmax_done"), sem("kbias_done")
        ek_done, ek_tok_done, krec_done = sem("ek_done"), sem("ek_tok_done"), sem("krec_done")
        qmax_done, q_sh_done, eq_done = sem("qmax_done"), sem("q_sh_done"), sem("eq_done")
        v_done, ctx_m_done, ctx_bd_done = sem("v_done"), sem("ctx_m_done"), sem("ctx_bd_done")
        qrec_done, y_done = sem("qrec_done"), sem("y_done")
        st2_done, mv2_done = sem("st2_done"), sem("mv2_done")
        ve2_done, rstd2_done, yhat_done = sem("ve2_done"), sem("rstd2_done"), sem("yhat_done")
        h_done, gob_done, xres_done = sem("h_done"), sem("gob_done"), sem("xres_done")
        s_f_done, s_hi_done, s_lo_done = sem("s_f_done"), sem("s_hi_done"), sem("s_lo_done")
        o_mm, o_g_done, res_done, stored = sem("o_mm"), sem("o_g_done"), sem("res_done"), sem("stored")

        x_dram = x.rearrange("b (p t) d -> p b t d", t=T)
        out_dram = out.rearrange("b (p t) d -> p b t d", t=T)

        block = ctx.enter_context(nc.Block())

        @block.sync
        def _(sp):
            sp.dma_start(x_all[:, 0, :, :], x_dram[:, 0, :, :]).then_inc(x0_in, 16)
            for n, w in (("k", wk), ("q", wq), ("v", wv)):
                sp.dma_start(w_raw[n][:, :, :], w.rearrange("(c p) n -> p c n", p=P)).then_inc(w_in[n], 16)
            sp.dma_start(x_all[:, 1, :, :], x_dram[:, 1, :, :]).then_inc(x1_in, 16)
            sp.dma_start(x_all[:, 2:B, :, :], x_dram[:, 2:B, :, :]).then_inc(xr_in, 16)
            sp.dma_start(emb_sb[:, :, :], emb_w.rearrange("(c p) n -> p c n", p=P)).then_inc(emb_in, 16)
            sp.dma_start(w_raw["o"][:, :, :], out_w.rearrange("(c p) n -> p c n", p=P)).then_inc(w_in["o"], 16)
            sp.dma_start(gate_bc[:, :, :].rearrange("p b d -> p (b d)"),
                         cond.rearrange("b d -> (b d)").partition_broadcast(P)).then_inc(gate_in, 16)
            sp.dma_start(outb_bc[:, :], out_b.partition_broadcast(P)).then_inc(gate_in, 16)
            with sp.Fori(0, B) as b:
                sp.wait_ge(res_done, b + 1)
                sp.dma_start(out_dram[:, b, :, :], x_all[:, b, :, :]).then_inc(stored, 16)
            sp.wait_ge(stored, 16 * B)

        @block.tensor
        def _(pe):
            mm = nc.tensor.matmul

            def three_passes(dst, lhs_hi, lhs_lo, rhs_hi, rhs_lo, last=True):
                passes = [(l, r, c) for c in range(C)
                          for l, r in ((lhs_hi, rhs_hi), (lhs_hi, rhs_lo), (lhs_lo, rhs_hi))]
                for n, (l, r, c) in enumerate(passes):
                    ins = mm(dst, l(c), r(c), start=(n == 0), stop=(last and n == len(passes) - 1))
                return ins

            def transpose_x(i):
                pe.wait_ge(xhat_done, i + 1)
                if not isinstance(i, int) or i >= 2:
                    pe.wait_ge(eq_done, i - 1)
                for c in range(C):
                    for t in range(T):
                        ins = nc.tensor.transpose(ps_x[:, c, t * P:(t + 1) * P],
                                                  xhat[:, t, c * P:(c + 1) * P], ident[:, :])
                ins.then_inc(xt_mm, 1)

            def project_k(i, par):
                pe.wait_ge(xt_hi_done, i + 1)
                pe.wait_ge(xt_lo_done, i + 1)
                if not isinstance(i, int) or i >= 1:
                    pe.wait_ge(h_done, i)
                for h in range(C):
                    cols = slice(h * P, (h + 1) * P)
                    ins = three_passes(ps_k[:, h, :],
                                       lambda c: w_hi["k"][:, c, cols], lambda c: w_lo["k"][:, c, cols],
                                       lambda c: xt_hi[:, par, c, :], lambda c: xt_lo[:, par, c, :])
                ins.then_inc(k_mm, 1)

            def project_q(i, par):
                if not isinstance(i, int) or i >= 1:
                    pe.wait_ge(q_sh_done, i)
                for t in range(T):
                    toks = slice(t * P, (t + 1) * P)
                    three_passes(ps_q[:, t, :],
                                 lambda c: xt_hi[:, par, c, toks], lambda c: xt_lo[:, par, c, toks],
                                 lambda c: w_hi["q"][:, c, :], lambda c: w_lo["q"][:, c, :], last=False)
                    if isinstance(i, int) and i == 0 and t == 0:
                        pe.wait_ge(bq_rows_done, 3)
                    ins = mm(ps_q[:, t, :], bias_sel[:, :], bq_rows[:, :], start=False, stop=True)
                ins.then_inc(q_mm, 1)

            def project_v(i, par):
                if not isinstance(i, int) or i >= 1:
                    pe.wait_ge(v_done, i)
                for t in range(T):
                    toks = slice(t * P, (t + 1) * P)
                    ins = three_passes(ps_v[:, t, :],
                                       lambda c: xt_hi[:, par, c, toks], lambda c: xt_lo[:, par, c, toks],
                                       lambda c: w_hi["v"][:, c, :], lambda c: w_lo["v"][:, c, :])
                ins.then_inc(v_mm, 1)

            def transpose_ek(i):
                pe.wait_ge(ek_done, 2 * (i + 1))
                if not isinstance(i, int) or i >= 1:
                    pe.wait_ge(ek_tok_done, i)
                for t in range(T):
                    for h in range(C):
                        ins = nc.tensor.transpose(ps_ek[:, t, h * P:(h + 1) * P],
                                                  ek[:, h, t * P:(t + 1) * P], ident[:, :])
                ins.then_inc(ekt_mm, 1)

            def transpose_q(i, last):
                pe.wait_ge(q_sh_done, i + 1)
                if not last:
                    pe.wait_ge(xt_lo_done, i + 2)
                for h in range(C):
                    for t in range(T):
                        ins = nc.tensor.transpose(ps_x[:, h, t * P:(t + 1) * P],
                                                  q_sh[:, t, h * P:(h + 1) * P], ident[:, :])
                ins.then_inc(qt_mm, 1)

            def context(i):
                pe.wait_ge(v_done, i + 1)
                pe.wait_ge(ek_tok_done, i + 1)
                if not isinstance(i, int) or i >= 1:
                    pe.wait_ge(ctx_m_done, 2 * i)
                for h in range(C):
                    cols = slice(h * P, (h + 1) * P)
                    for t in range(T):
                        ins = mm(ps_c[:, h, 0:P], ek_tok[:, t, cols], v_tok[:, t, cols],
                                 start=(t == 0), stop=(t == T - 1))
                ins.then_inc(ctx_mm, 1)

            def attend(i):
                pe.wait_ge(eq_done, i + 1)
                pe.wait_ge(ctx_bd_done, i + 1)
                for t in range(T):
                    for h in range(C):
                        ins = mm(ps_y[:, t, h * HC * W:(h + 1) * HC * W], eq[:, h, t * P:(t + 1) * P],
                                 ctx_bd[:, h, :, :], start=True, stop=True)
                ins.then_inc(y_mm, 1)

            def transpose_y(i, last=False):
                pe.wait_ge(yhat_done, 2 * (i + 1))
                if not last:
                    pe.wait_ge(ek_done, 2 * (i + 2))
                for h in range(C):
                    for t in range(T):
                        ins = nc.tensor.transpose(ps_k[:, h, t * P:(t + 1) * P],
                                                  yhat[:, t, h * P:(h + 1) * P], ident[:, :])
                ins.then_inc(yt_mm, 1)

            def step(i, par, first=False, last=False):
                project_k(i, par)
                if not first:
                    attend(i - 1)
                project_q(i, par)
                if not last:
                    transpose_x(i + 1)
                project_v(i, par)
                transpose_ek(i)
                if not first:
                    transpose_y(i - 1)
                transpose_q(i, last)
                context(i)

            def project_out(b, par):
                pe.wait_ge(s_hi_done, b + 1)
                pe.wait_ge(s_lo_done, b + 1)
                if not isinstance(b, int) or b >= 2:
                    pe.wait_ge(o_g_done, b - 1)
                for t in range(T):
                    toks = slice(t * P, (t + 1) * P)
                    ins = three_passes(ps_y[:, par, t * D:(t + 1) * D],
                                       lambda c: s_hi[:, par, c, toks], lambda c: s_lo[:, par, c, toks],
                                       lambda c: w_hi["o"][:, c, :], lambda c: w_lo["o"][:, c, :])
                ins.then_inc(o_mm, 1)

            pe.wait_ge(ident_done, 2)
            pe.wait_ge(vec_in, 16 * 7)
            nc.tensor.transpose(ps_c[:, 0, 0:NV], vec_rows[:, :], ident[0:NV, 0:NV]).then_inc(vec_t_done, 1)
            transpose_x(0)
            pe.wait_ge(vec_done, 1)
            pe.wait_ge(w_in["k"], 16)
            for h in range(C):
                for c in range(C):
                    ins = mm(ps_c[:, 1, h:h + 1], w_raw["k"][:, c, h * P:(h + 1) * P], b_v[:, c:c + 1],
                             start=(c == 0), stop=(c == C - 1))
            ins.then_inc(ck_mm_done, 1)
            pe.wait_ge(row_in, 32)
            pe.wait_ge(const_done, 2)
            for k, n in enumerate("qv"):
                pe.wait_ge(w_in[n], 16)
                for c in range(C):
                    mm(ps_y[:, 0, k * D:(k + 1) * D], b_v[:, c:c + 1].to_broadcast([P, P]),
                       w_raw[n][:, c, :], start=(c == 0), stop=False)
                ins = mm(ps_y[:, 0, k * D:(k + 1) * D], ones[0:1, :], bqv_row[:, k, :], start=False, stop=True)
            ins.then_inc(cqv_mm_done, 1)
            pe.wait_ge(w_lo_done, 2)
            pe.wait_ge(w_hi_done, 2)
            project_k(0, 0)
            pe.wait_ge(w_lo_done, 4)
            project_q(0, 0)
            transpose_x(1)
            pe.wait_ge(w_lo_done, 6)
            project_v(0, 0)
            pe.wait_ge(silu_c_done, 1)
            pe.wait_ge(emb_in, 16)
            for j in range(2 * C):
                for c in range(C):
                    ins = mm(ps_y[:, 1, j * B:(j + 1) * B], emb_sb[:, c, j * P:(j + 1) * P],
                             silu_c[:, c, :], start=(c == 0), stop=(c == C - 1))
            ins.then_inc(emb_mm_done, 1)
            transpose_ek(0)
            transpose_q(0, False)
            pe.wait_ge(ck_done, 1)
            context(0)

            with pe.Fori(1, B - 2, 2) as i:
                step(i, 1)
                step(i + 1, 0)
            step(B - 1, 1, last=True)
            attend(B - 1)
            pe.wait_ge(w_lo_done, 7)
            pe.wait_ge(y_done, B)
            project_out(0, 0)
            project_out(1, 1)
            transpose_y(B - 1, last=True)
            with pe.Fori(2, B - 1, 2) as b:
                project_out(b, 0)
                project_out(b + 1, 1)

        @block.vector
        def _(dve):
            def row_stats(i):
                if isinstance(i, int) and i < 3:
                    dve.wait_ge((x0_in, x1_in, xr_in)[i], 16)
                for t in range(T):
                    dve.bn_stats(st1[:, t, :], x_all[:, i, t, :]).then_inc(st1_done, 1)
                dve.drain()
                for t in range(T):
                    dve.bn_aggr(mv1[:, t, :], st1[:, t, :]).then_inc(mv1_done, 1)
                dve.wait_ge(mv1_done, 2 * (i + 1))
                dve.tensor_scalar(ve1[:, :], mv1[:, :, 1], EPS, None, ALU.add).then_inc(ve1_done, 1)

            def normalise_x(i):
                dve.wait_ge(rstd1_done, i + 1)
                if not isinstance(i, int) or i >= 1:
                    dve.wait_ge(xt_mm, i)
                for t in range(T):
                    ins = dve.tensor_scalar(xhat[:, t, :], x_all[:, i, t, :], mv1[:, t, 0:1],
                                            rstd1[:, t:t + 1], ALU.subtract, ALU.mult)
                ins.then_inc(xhat_done, 1)

            def split_x(i, par):
                dve.wait_ge(xt_hi_done, i + 1)
                dve.tensor_tensor(xt_lo[:, par, :, :], ps_x[:, :, :], xt_hi[:, par, :, :].bitcast(F32),
                                  ALU.subtract).then_inc(xt_lo_done, 1)

            def k_bias(i):
                dve.wait_ge(k_mm, i + 1)
                dve.tensor_reduce(kmax0[:, :], ps_k[:, :, :], AX.X, ALU.max).then_inc(kmax0_done, 1)
                dve.wait_ge(kmax0_done, i + 1)
                dve.tensor_tensor(kmax[:, :], kmax0[:, :], ck_sb[:, :], ALU.add).then_inc(kmax_done, 1)
                dve.wait_ge(kmax_done, i + 1)
                dve.tensor_tensor(kbias[:, :], ck_sb[:, :], kmax[:, :], ALU.subtract).then_inc(kbias_done, 1)

            def shift_q(i):
                dve.wait_ge(q_mm, i + 1)
                dve.tensor_reduce(qmax[:, :, :], ps_q[:, :, :].rearrange("p t (h d) -> p t h d", d=DH),
                                  AX.X, ALU.max).then_inc(qmax_done, 1)
                dve.wait_ge(qmax_done, i + 1)
                dve.tensor_tensor(q_sh[:, :, :].rearrange("p t (h d) -> p (t h) d", d=DH),
                                  ps_q[:, :, :].rearrange("p t (h d) -> p (t h) d", d=DH),
                                  qmax[:, :, :].rearrange("p t h -> p (t h)").unsqueeze(2)
                                  .to_broadcast([P, T * HEADS, DH]),
                                  ALU.subtract).then_inc(q_sh_done, 1)

            def k_reciprocal(i):
                dve.wait_ge(ek_done, 2 * (i + 1))
                dve.reciprocal(krec[:, :], ksum[:, :]).then_inc(krec_done, 1)

            def mask_context(i):
                dve.wait_ge(ctx_mm, i + 1)
                dve.wait_ge(krec_done, i + 1)
                for h in range(C):
                    dve.scalar_tensor_tensor(out=ctx_m[:, h, :, :],
                                             in0=ps_c[:, h, 0:P].rearrange("p (j d) -> p j d", d=DH),
                                             scalar=krec[:, h:h + 1], in1=head_mask[:, :, 0:DH],
                                             op0=ALU.mult, op1=ALU.mult).then_inc(ctx_m_done, 1)

            def scale_y(i):
                dve.wait_ge(y_mm, i + 1)
                heads = ps_y[:, :, 0:HEADS * W].rearrange("p t (h w) -> p t h w", w=W)
                dve.reciprocal(qrec[:, :, :], heads[:, :, :, DH]).then_inc(qrec_done, 1)
                dve.wait_ge(qrec_done, i + 1)
                dve.tensor_tensor(y[:, :, :].rearrange("p t (h d) -> p t h d", d=DH), heads[:, :, :, 0:DH],
                                  qrec[:, :, :].unsqueeze(3).to_broadcast([P, T, HEADS, DH]),
                                  ALU.mult).then_inc(y_done, 1)
                dve.wait_ge(y_done, i + 1)
                for t in range(T):
                    dve.bn_stats(st2[:, t, :], y[:, t, :]).then_inc(st2_done, 1)
                dve.drain()
                for t in range(T):
                    dve.bn_aggr(mv2[:, t, :], st2[:, t, :]).then_inc(mv2_done, 1)
                dve.wait_ge(mv2_done, 2 * (i + 1))
                dve.tensor_scalar(ve2[:, :], mv2[:, :, 1], EPS, None, ALU.add).then_inc(ve2_done, 1)

            def normalise_y(i):
                dve.wait_ge(rstd2_done, i + 1)
                for t in range(T):
                    dve.tensor_scalar(yhat[:, t, :], y[:, t, :], mv2[:, t, 0:1], rstd2[:, t:t + 1],
                                      ALU.subtract, ALU.mult).then_inc(yhat_done, 1)

            def step(i, par, first=False, last=False, x2=True):
                if not first:
                    mask_context(i - 1)
                if not last:
                    normalise_x(i + 1)
                k_bias(i)
                if not first:
                    scale_y(i - 1)
                shift_q(i)
                if not last:
                    split_x(i + 1, 1 - par)
                if not first:
                    normalise_y(i - 1)
                k_reciprocal(i)
                if x2:
                    row_stats(i + 2)

            def split_s(b, par):
                dve.wait_ge(s_f_done, b + 1)
                dve.wait_ge(s_hi_done, b + 1)
                if not isinstance(b, int) or b >= 2:
                    dve.wait_ge(o_mm, b - 1)
                dve.tensor_tensor(s_lo[:, par, :, :], s_f[:, par, :, :], s_hi[:, par, :, :].bitcast(F32),
                                  ALU.subtract).then_inc(s_lo_done, 1)

            def gate_o(b, par):
                dve.wait_ge(o_mm, b + 1)
                if not isinstance(b, int) or b >= 2:
                    dve.wait_ge(res_done, b - 1)
                dve.tensor_tensor(o_g[:, par, :, :], ps_y[:, par, :].rearrange("p (t d) -> p t d", d=D),
                                  gate_bc[:, b, :].unsqueeze(1).to_broadcast([P, T, D]),
                                  ALU.mult).then_inc(o_g_done, 1)

            row_stats(0)
            dve.wait_ge(vec_t_done, 1)
            dve.tensor_copy(vec[:, :], ps_c[:, 0, 0:NV]).then_inc(vec_done, 1)
            normalise_x(0)
            dve.wait_ge(vec_done, 1)

            def weight_lo(n, k):
                for c in range(C):
                    dve.wait_ge(w_hi_done, 2 * k + c + 1)
                    dve.scalar_tensor_tensor(out=w_lo[n][:, c, :], in0=w_raw[n][:, c, :], scalar=g_v[:, c:c + 1],
                                             in1=w_hi[n][:, c, :].bitcast(F32), op0=ALU.mult,
                                             op1=ALU.subtract).then_inc(w_lo_done, 1)

            weight_lo("k", 0)
            split_x(0, 0)
            weight_lo("q", 1)
            dve.wait_ge(ck_mm_done, 1)
            dve.tensor_tensor(ck_sb[:, :], ps_c[:, 1, 0:C], bk_v, ALU.add).then_inc(ck_done, 1)
            dve.wait_ge(cqv_mm_done, 1)
            dve.tensor_copy(cqv_sb[:, :, :], ps_y[:, 0, :].rearrange("p (k d) -> p k d", k=2)).then_inc(cqv_done, 1)
            dve.wait_ge(cqv_done, 1)
            dve.tensor_copy(bq_rows[0:64, :], cqv_sb[0:64, 0, :]).then_inc(bq_rows_done, 1)
            dve.tensor_copy(y[64:P, 0, :].bitcast(F32R), cqv_sb[64:P, 0, :]).then_inc(small_done, 1)
            dve.wait_ge(small_done, 1)
            dve.tensor_tensor(bq_rows[64:P, :], cqv_sb[64:P, 0, :], y[64:P, 0, :],
                              ALU.subtract).then_inc(bq_rows_done, 1)
            row_stats(1)
            weight_lo("v", 2)
            dve.wait_ge(ck_done, 1)
            normalise_x(1)
            k_bias(0)
            dve.wait_ge(silu_e_done, 1)
            dve.tensor_scalar(silu_1e[:, :, :], silu_e[:, :, :], 1.0, None, ALU.add).then_inc(small_done, 1)
            dve.wait_ge(small_done, 2)
            dve.reciprocal(silu_r[:, :, :], silu_1e[:, :, :]).then_inc(small_done, 1)
            dve.wait_ge(small_done, 3)
            dve.tensor_tensor(silu_c[:, :, :], silu_r[:, :, :], cond_v, ALU.mult).then_inc(silu_c_done, 1)
            shift_q(0)
            split_x(1, 1)
            k_reciprocal(0)
            row_stats(2)
            dve.wait_ge(mask_done, 3)
            for h in range(C):
                ins = dve.tensor_tensor(cv_blk[:, h, :, :],
                                        cqv_sb[:, 1, h * P:(h + 1) * P].rearrange("p (j d) -> p j d", d=DH),
                                        head_mask[:, :, 0:DH], ALU.mult)
            ins.then_inc(cv_done, 1)
            dve.wait_ge(emb_mm_done, 1)
            dve.tensor_tensor(emb_o[:, :, :], ps_y[:, 1, 0:2 * C * B].rearrange("p (j b) -> p j b", b=B),
                              embb_v.unsqueeze(2).to_broadcast([P, 2 * C, B]), ALU.add).then_inc(small_done, 1)
            dve.wait_ge(small_done, 4)
            dve.tensor_scalar(scale1[:, :, :], emb_o[:, 0:C, :], 1.0, None, ALU.add).then_inc(small_done, 1)
            dve.wait_ge(small_done, 5)
            dve.tensor_tensor(h_scale[:, :, :].rearrange("p b c -> p c b"), scale1[:, :, :],
                              sng_v.unsqueeze(2).to_broadcast([P, C, B]), ALU.mult).then_inc(affine_done, 1)
            dve.tensor_tensor(shift_t[:, :, :], scale1[:, :, :],
                              snb_v.unsqueeze(2).to_broadcast([P, C, B]), ALU.mult).then_inc(small_done, 1)
            dve.wait_ge(small_done, 6)
            dve.tensor_tensor(h_bias[:, :, :].rearrange("p b c -> p c b"), shift_t[:, :, :],
                              emb_o[:, C:2 * C, :], ALU.add).then_inc(affine_done, 1)

            dve_last = B - 1
            with dve.Fori(1, B - 4, 2) as i:
                step(i, 1)
                step(i + 1, 0)
            step(B - 3, 1)
            step(B - 2, 0, x2=False)
            step(dve_last, 1, last=True, x2=False)
            mask_context(dve_last)
            scale_y(dve_last)
            dve.wait_ge(gate_in, 32)
            split_s(0, 0)
            normalise_y(dve_last)
            split_s(1, 1)
            gate_o(0, 0)
            gate_o(1, 1)
            with dve.Fori(2, B - 1, 2) as b:
                for par in (0, 1):
                    split_s(b + par, par)
                    gate_o(b + par, par)

        @block.scalar
        def _(act):
            def hi_x(i, par):
                act.wait_ge(xt_mm, i + 1)
                if not isinstance(i, int) or i >= 2:
                    act.wait_ge(v_mm, i - 1)
                nc.scalar.activation(xt_hi[:, par, :, :], ps_x[:, :, :], ACT.Identity).then_inc(xt_hi_done, 1)

            def exp_k(i):
                act.wait_ge(kbias_done, i + 1)
                if not isinstance(i, int) or i >= 1:
                    act.wait_ge(ekt_mm, i)
                    act.wait_ge(krec_done, i)
                for h in range(C):
                    nc.scalar.activation(ek[:, h, :], ps_k[:, h, :], ACT.Exp, bias=kbias[:, h:h + 1],
                                         accum_out=ksum[:, h:h + 1]).then_inc(ek_done, 1)

            def copy_v(i):
                act.wait_ge(v_mm, i + 1)
                if not isinstance(i, int) or i >= 1:
                    act.wait_ge(ctx_mm, i)
                nc.scalar.activation(v_tok[:, :, :], ps_v[:, :, :], ACT.Identity).then_inc(v_done, 1)

            def copy_ek(i):
                act.wait_ge(ekt_mm, i + 1)
                nc.scalar.activation(ek_tok[:, :, :], ps_ek[:, :, :], ACT.Identity).then_inc(ek_tok_done, 1)

            def affine_y(i):
                act.wait_ge(yt_mm, i + 1)
                for h in range(C):
                    ins = nc.scalar.activation(h_all[:, i, h, :], ps_k[:, h, :], ACT.Identity,
                                               scale=h_scale[:, i, h:h + 1], bias=h_bias[:, i, h:h + 1])
                ins.then_inc(h_done, 1)

            def exp_q(i):
                act.wait_ge(qt_mm, i + 1)
                if not isinstance(i, int) or i >= 1:
                    act.wait_ge(y_mm, i)
                nc.scalar.activation(eq[:, :, :], ps_x[:, :, :], ACT.Exp).then_inc(eq_done, 1)

            def step(i, par, first=False, last=False):
                exp_k(i)
                if not last:
                    hi_x(i + 1, 1 - par)
                copy_v(i)
                copy_ek(i)
                if not first:
                    affine_y(i - 1)
                exp_q(i)

            def silu(b, par):
                if not isinstance(b, int) or b >= 2:
                    act.wait_ge(s_lo_done, b - 1)
                    act.wait_ge(o_mm, b - 1)
                nc.scalar.activation(s_f[:, par, :, :], h_all[:, b, :, :], ACT.Silu).then_inc(s_f_done, 1)
                nc.scalar.activation(s_hi[:, par, :, :], h_all[:, b, :, :], ACT.Silu).then_inc(s_hi_done, 1)

            for k, (n, v) in enumerate((("g", norm_g), ("b", norm_b), ("k", bk), ("sg", sn_g), ("sb", sn_b))):
                at_row = 2 * B + 2 * k
                act.dma_start(vec_rows[at_row:at_row + 2, :], v.rearrange("(c p) -> c p", p=P)).then_inc(vec_in, 16)
            act.dma_start(vec_rows[2 * B + 10:NV, :], emb_b.rearrange("(c p) -> c p", p=P)).then_inc(vec_in, 16)
            act.dma_start(vec_rows[0:2 * B, :], cond.rearrange("b (c p) -> (b c) p", p=P)).then_inc(vec_in, 16)
            act.dma_start(bqv_row[:, 0, :], bq.unsqueeze(0)).then_inc(row_in, 16)
            act.dma_start(bqv_row[:, 1, :], bv.unsqueeze(0)).then_inc(row_in, 16)
            act.wait_ge(vec_done, 1)

            def weight_hi(n):
                act.wait_ge(w_in[n], 16)
                for c in range(C):
                    nc.scalar.activation(w_hi[n][:, c, :], w_raw[n][:, c, :], ACT.Identity,
                                         scale=g_v[:, c:c + 1]).then_inc(w_hi_done, 1)

            weight_hi("k")
            hi_x(0, 0)
            weight_hi("q")
            weight_hi("v")
            nc.scalar.activation(silu_e[:, :, :], cond_v, ACT.Exp, scale=-1.0).then_inc(silu_e_done, 1)
            exp_k(0)
            hi_x(1, 1)
            copy_v(0)
            copy_ek(0)
            exp_q(0)
            act.wait_ge(w_in["o"], 16)
            for c, done in enumerate((h_done, w_hi_done)):
                nc.scalar.activation(w_hi["o"][:, c, :], w_raw["o"][:, c, :], ACT.Identity).then_inc(done, 1)
            act.wait_ge(affine_done, 2)
            with act.Fori(1, B - 2, 2) as i:
                step(i, 1)
                step(i + 1, 0)
            step(B - 1, 1, last=True)
            act.wait_ge(h_done, B)
            silu(0, 0)
            silu(1, 1)
            affine_y(B - 1)
            act.wait_ge(h_done, B + 1)
            with act.Fori(2, B - 1, 2) as b:
                silu(b, 0)
                silu(b + 1, 1)

        @block.gpsimd
        def _(pool):
            def power(rstd, ve):
                return nc.gpsimd.tensor_tensor(rstd[:, :], ve[:, :], minus_half[:, :], ALU.pow)

            def rstd_x(i):
                pool.wait_ge(ve1_done, i + 1)
                if not isinstance(i, int) or i >= 1:
                    pool.wait_ge(xhat_done, i)
                power(rstd1, ve1).then_inc(rstd1_done, 1)

            def rstd_y(i):
                pool.wait_ge(ve2_done, i + 1)
                power(rstd2, ve2).then_inc(rstd2_done, 1)

            def finish_context(i):
                pool.wait_ge(ctx_m_done, 2 * (i + 1))
                for h in range(C):
                    ins = nc.gpsimd.tensor_tensor(ctx_bd[:, h, :, 0:DH], ctx_m[:, h, :, :],
                                                  cv_blk[:, h, :, :], ALU.add)
                ins.then_inc(ctx_bd_done, 1)

            def residual(i):
                pool.wait_ge(xhat_done, i + 1)
                if not isinstance(i, int) or i >= 1:
                    pool.wait_ge(xres_done, i)
                nc.gpsimd.tensor_tensor(gob[:, :], gate_bc[:, i, :], outb_bc[:, :], ALU.mult).then_inc(gob_done, 1)
                pool.wait_ge(gob_done, i + 1)
                nc.gpsimd.tensor_tensor(x_all[:, i, :, :], x_all[:, i, :, :],
                                        gob[:, :].unsqueeze(1).to_broadcast([P, T, D]),
                                        ALU.add).then_inc(xres_done, 1)

            def step(i, x2=True):
                finish_context(i - 1)
                residual(i)
                rstd_y(i - 1)
                if x2:
                    rstd_x(i + 2)

            def add_residual(b, par):
                pool.wait_ge(o_g_done, b + 1)
                nc.gpsimd.tensor_tensor(x_all[:, b, :, :], o_g[:, par, :, :], x_all[:, b, :, :],
                                        ALU.add).then_inc(res_done, 1)

            nc.gpsimd.memset(minus_half[:, :], -0.5).then_inc(const_done, 1)
            nc.gpsimd.memset(ident[:, :], 0.0).then_inc(ident_done, 1)
            pool.wait_ge(ident_done, 1)
            nc.gpsimd.affine_select(out=ident[:, :], in_=ident[:, :], compare_op=ALU.not_equal, fill=1.0, base=0,
                                    pattern=[[-1, P]], channel_multiplier=1).then_inc(ident_done, 1)
            nc.gpsimd.memset(ones[:, :], 1.0).then_inc(const_done, 1)
            pool.wait_ge(const_done, 2)
            rstd_x(0)
            nc.gpsimd.affine_select(out=bias_self[:, :], in_=ones[:, :], compare_op=ALU.is_equal, fill=0.0, base=0,
                                    pattern=[[0, P]], channel_multiplier=1).then_inc(blank_done, 1)
            pool.wait_ge(blank_done, 1)
            nc.gpsimd.affine_select(out=bias_sel[:, :], in_=bias_self[:, :], compare_op=ALU.not_equal, fill=1.0,
                                    base=-64, pattern=[[0, P]], channel_multiplier=1).then_inc(bq_rows_done, 1)
            rstd_x(1)
            nc.gpsimd.memset(head_mask[:, :, :], 1.0).then_inc(mask_done, 1)
            pool.wait_ge(mask_done, 1)
            for n, (sign, base) in enumerate(((1, 0), (-1, DH - 1))):
                nc.gpsimd.affine_select(out=head_mask[:, :, :], in_=head_mask[:, :, :], compare_op=ALU.is_ge,
                                        fill=0.0, base=base, pattern=[[-sign * DH, HC], [0, W]],
                                        channel_multiplier=sign).then_inc(mask_done, 1)
                pool.wait_ge(mask_done, n + 2)
            for h in range(C):
                nc.gpsimd.tensor_copy(ctx_bd[:, h, :, DH:W], head_mask[:, :, DH:W]).then_inc(const_done, 1)
            pool.wait_ge(const_done, 4)
            rstd_x(2)
            pool.wait_ge(w_hi_done, 7)
            nc.gpsimd.tensor_tensor(w_lo["o"][:, :, :], w_raw["o"][:, :, :], w_hi["o"][:, :, :].bitcast(F32),
                                    ALU.subtract).then_inc(w_lo_done, 1)
            pool.wait_ge(gate_in, 32)
            residual(0)
            pool.wait_ge(cv_done, 1)
            with pool.Fori(1, B - 2) as i:
                step(i)
            step(B - 2, x2=False)
            step(B - 1, x2=False)
            finish_context(B - 1)
            rstd_y(B - 1)
            pool.wait_ge(xres_done, B)
            with pool.Fori(0, B - 1, 2) as b:
                add_residual(b, 0)
                add_residual(b + 1, 1)


_INS = ["x", "cond_1024"] + ["L0_cond_" + n for n in (
    "norm_g", "norm_b", "Wq", "bq", "Wk", "bk", "Wv", "bv", "emb_W", "emb_b", "sn_g", "sn_b", "out_W", "out_b")]


def kernel(**inputs):
    import concourse.bacc as bacc
    from concourse.bass_utils import run_bass_kernel_spmd

    nc = bacc.Bacc("TRN2", target_bir_lowering=False, num_devices=1)
    arrays, args = {}, []
    for name in _INS:
        a = np.ascontiguousarray(inputs[name])
        arrays[f"in_{name}"] = a
        args.append(nc.dram_tensor(f"in_{name}", a.shape, mybir.dt.from_np(a.dtype), kind="ExternalInput").ap())
    shape = arrays["in_x"].shape
    args.append(nc.dram_tensor("out_0", shape, F32, kind="ExternalOutput").ap())
    linear_attention_block(nc, *args)
    r = run_bass_kernel_spmd(nc, [arrays], core_ids=[0])
    return r.results[0]["out_0"]
```

```python
from contextlib import ExitStack

import numpy as np

import concourse.bass as bass
from concourse import mybir

F32 = mybir.dt.float32
F32R = mybir.dt.float32r
ALU = mybir.AluOpType
ACT = mybir.ActivationFunctionType
AX = mybir.AxisListType

P = 128
HEADS = 16
EPS = 1e-5


def linear_attention_block(nc, x, cond, wq, wk, wv, emb_w, out_w, out_b, vectors, bqv, out):
    B, N, D = x.shape
    T, C = N // P, D // P
    DH = D // HEADS
    HC = P // DH
    W = DH + 1
    assert T == 2 and C == 2 and B % 2 == 0 and B >= 8

    ctx = ExitStack()
    with ctx:
        def sb(name, shape, dt=F32):
            return ctx.enter_context(nc.sbuf_tensor(name, shape, dt))

        def psum(name, shape):
            return ctx.enter_context(nc.psum_tensor(name, shape, F32))

        def sem(name):
            return ctx.enter_context(nc.semaphore(name))

        w_raw = {n: sb(f"w{n}_raw", [P, C, D]) for n in "qkvo"}
        w_hi = {n: sb(f"w{n}_hi", [P, C, D], F32R) for n in "qkvo"}
        w_lo = {n: sb(f"w{n}_lo", [P, C, D], F32R) for n in "qkvo"}
        emb_sb = sb("emb_sb", [P, C, 2 * D])
        NV = 2 * B + 14
        vec = sb("vec", [P, NV])
        at = 2 * B
        cond_v = vec[:, 0:at].rearrange("p (b c) -> p c b", c=C)
        g_v, b_v, bk_v, sng_v, snb_v = (vec[:, at + 2 * k:at + 2 * k + 2] for k in range(5))
        embb_v = vec[:, at + 10:at + 14]
        bqv_row = sb("bqv_row", [1, 2, D])
        outb_bc = sb("outb_bc", [P, D])
        gate_bc = sb("gate_bc", [P, B, D])
        ident = sb("ident", [P, P])
        ones = sb("ones", [P, P])
        head_mask = sb("head_mask", [P, HC, W])
        minus_half = sb("minus_half", [P, 2])
        bias_sel = sb("bias_sel", [P, P], F32R)
        bias_row0 = sb("bias_row0", [P, P])
        bq_rows = sb("bq_rows", [P, D], F32R)
        bq_hi = sb("bq_hi", [P, D], F32R)
        ck_sb = sb("ck_sb", [P, C])
        cv_blk = sb("cv_blk", [P, C, HC, DH])
        silu_e = sb("silu_e", [P, C, B])
        silu_1e = sb("silu_1e", [P, C, B])
        silu_r = sb("silu_r", [P, C, B])
        silu_c = sb("silu_c", [P, C, B])
        emb_o = sb("emb_o", [P, 2 * C, B])
        scale1 = sb("scale1", [P, C, B])
        shift_t = sb("shift_t", [P, C, B])
        h_scale = sb("h_scale", [P, B, C])
        h_bias = sb("h_bias", [P, B, C])

        x_all = sb("x_all", [P, B, T, D])
        h_all = sb("h_all", [P, B, C, N])
        st1 = sb("st1", [P, T, 6])
        mv1 = sb("mv1", [P, T, 2])
        ve1 = sb("ve1", [P, T])
        rstd1 = sb("rstd1", [P, T])
        nmr1 = sb("nmr1", [P, T])
        xhat = sb("xhat", [P, T, D])
        xt_hi = sb("xt_hi", [P, 2, C, N], F32R)
        xt_lo = sb("xt_lo", [P, 2, C, N], F32R)
        kmax0 = sb("kmax0", [P, C])
        kmax = sb("kmax", [P, C])
        kbias = sb("kbias", [P, C])
        ksum = sb("ksum", [P, C])
        krec = sb("krec", [P, C])
        ek = sb("ek", [P, C, N])
        ek_tok = sb("ek_tok", [P, T, D])
        qmax = sb("qmax", [P, T, HEADS])
        q_sh = sb("q_sh", [P, T, D])
        eq = sb("eq", [P, C, N])
        v_tok = sb("v_tok", [P, T, D])
        ctx_m = sb("ctx_m", [P, C, HC, DH])
        ctx_bd = sb("ctx_bd", [P, C, HC, W])
        qrec = sb("qrec", [P, T, HEADS])
        y = sb("y", [P, T, D])
        st2 = sb("st2", [P, T, 6])
        mv2 = sb("mv2", [P, T, 2])
        ve2 = sb("ve2", [P, T])
        rstd2 = sb("rstd2", [P, T])
        yhat = sb("yhat", [P, T, D])
        gob = sb("gob", [P, D])
        s_f = sb("s_f", [P, B, C, N])
        s_hi = sb("s_hi", [P, B, C, N], F32R)
        s_lo = sb("s_lo", [P, B, C, N], F32R)
        o_g = sb("o_g", [P, 2, T, D])

        ps_x = psum("ps_x", [P, C, N])
        ps_k = psum("ps_k", [P, C, N])
        ps_q = psum("ps_q", [P, T, D])
        ps_v = psum("ps_v", [P, T, D])
        ps_t = psum("ps_t", [P, T, D])
        ps_cb = psum("ps_cb", [P, 512])
        ps_c = ps_cb[:, 0:C * P].rearrange("p (c n) -> p c n", c=C)
        ps_y = psum("ps_y", [P, 2, 512])
        ps_o = (ps_q, ps_v)

        x_in = [sem("x0_in"), sem("x1_in"), sem("x_rest_in")]
        w_in = {n: sem(f"w{n}_in") for n in "qkvo"}
        vec_in, row_in, gate_in, emb_in = sem("vec_in"), sem("row_in"), sem("gate_in"), sem("emb_in")
        row0_done = sem("row0_done")
        ident_done, mask_done, const_done = sem("ident_done"), sem("mask_done"), sem("const_done")
        w_hi_done, w_lo_done = sem("w_hi_done"), sem("w_lo_done")
        ck_mm_done, cqv_mm_done, emb_mm_done = sem("ck_mm_done"), sem("cqv_mm_done"), sem("emb_mm_done")
        ck_done, bq_rows_done = sem("ck_done"), sem("bq_rows_done")
        cv_done, silu_e_done, silu_c_done = sem("cv_done"), sem("silu_e_done"), sem("silu_c_done")
        small_done, affine_done = sem("small_done"), sem("affine_done")
        xt_mm, k_mm, q_mm, v_mm = sem("xt_mm"), sem("k_mm"), sem("q_mm"), sem("v_mm")
        ekt_mm, qt_mm, ctx_mm, y_mm, yt_mm = (sem(n) for n in ("ekt_mm", "qt_mm", "ctx_mm", "y_mm", "yt_mm"))
        st1_done, mv1_done = sem("st1_done"), sem("mv1_done")
        ve1_done, rstd1_done, xhat_done = sem("ve1_done"), sem("rstd1_done"), sem("xhat_done")
        nmr1_done = sem("nmr1_done")
        xt_hi_done, xt_lo_done = sem("xt_hi_done"), sem("xt_lo_done")
        kmax0_done, kmax_done, kbias_done = sem("kmax0_done"), sem("kmax_done"), sem("kbias_done")
        ek_done, ek_tok_done, krec_done = sem("ek_done"), sem("ek_tok_done"), sem("krec_done")
        qmax_done, q_sh_done, eq_done = sem("qmax_done"), sem("q_sh_done"), sem("eq_done")
        v_done, ctx_m_done, ctx_bd_done = sem("v_done"), sem("ctx_m_done"), sem("ctx_bd_done")
        qrec_done, y_done = sem("qrec_done"), sem("y_done")
        st2_done, mv2_done = sem("st2_done"), sem("mv2_done")
        ve2_done, rstd2_done, yhat_done = sem("ve2_done"), sem("rstd2_done"), sem("yhat_done")
        h_done, gob_done, xres_done = sem("h_done"), sem("gob_done"), sem("xres_done")
        s_f_done, s_hi_done, s_lo_done = sem("s_f_done"), sem("s_hi_done"), sem("s_lo_done")
        o_mm, o_g_done, res_done, stored = sem("o_mm"), sem("o_g_done"), sem("res_done"), sem("stored")

        x_dram = x.rearrange("b (p t) d -> p b t d", t=T)
        out_dram = out.rearrange("b (p t) d -> p b t d", t=T)

        block = ctx.enter_context(nc.Block())

        @block.sync
        def _(sp):
            sp.dma_start(x_all[:, 0, :, :], x_dram[:, 0, :, :]).then_inc(x_in[0], 16)
            sp.dma_start(w_raw["k"][:, :, :], wk.rearrange("(c p) n -> p c n", p=P)).then_inc(w_in["k"], 16)
            sp.dma_start(x_all[:, 1, :, :], x_dram[:, 1, :, :]).then_inc(x_in[1], 16)
            for n, w in (("v", wv), ("q", wq)):
                sp.dma_start(w_raw[n][:, :, :], w.rearrange("(c p) n -> p c n", p=P)).then_inc(w_in[n], 16)
            sp.dma_start(emb_sb[:, :, :], emb_w.rearrange("(c p) n -> p c n", p=P)).then_inc(emb_in, 16)
            sp.dma_start(x_all[:, 2:B, :, :], x_dram[:, 2:B, :, :]).then_inc(x_in[2], 16)
            sp.dma_start(w_raw["o"][:, :, :], out_w.rearrange("(c p) n -> p c n", p=P)).then_inc(w_in["o"], 16)
            sp.dma_start(gate_bc[:, :, :].rearrange("p b d -> p (b d)"),
                         cond.rearrange("b d -> (b d)").partition_broadcast(P)).then_inc(gate_in, 16)
            sp.dma_start(outb_bc[:, :], out_b.partition_broadcast(P)).then_inc(gate_in, 16)
            with sp.Fori(0, B) as b:
                sp.wait_ge(res_done, b + 1)
                sp.dma_start(out_dram[:, b, :, :], x_all[:, b, :, :]).then_inc(stored, 16)
            sp.wait_ge(stored, 16 * B)

        @block.tensor
        def _(pe):
            mm = nc.tensor.matmul

            def three_passes(dst, lhs_hi, lhs_lo, rhs_hi, rhs_lo, last=True):
                passes = [(l, r, c) for c in range(C)
                          for l, r in ((lhs_hi, rhs_hi), (lhs_hi, rhs_lo), (lhs_lo, rhs_hi))]
                for n, (l, r, c) in enumerate(passes):
                    ins = mm(dst, l(c), r(c), start=(n == 0), stop=(last and n == len(passes) - 1))
                return ins

            def keep_busy(n):
                for _ in range(n):
                    mm(ps_k[:, 0, 0:P], ones[:, :], ones[:, :], start=True, stop=True)

            def transpose_x(i):
                pe.wait_ge(xhat_done, i + 1)
                if not isinstance(i, int) or i >= 2:
                    pe.wait_ge(eq_done, i - 1)
                for c in range(C):
                    for t in range(T):
                        ins = nc.tensor.transpose(ps_x[:, c, t * P:(t + 1) * P],
                                                  xhat[:, t, c * P:(c + 1) * P], ident[:, :])
                ins.then_inc(xt_mm, 1)

            def project_k(i, par):
                pe.wait_ge(xt_hi_done, i + 1)
                pe.wait_ge(xt_lo_done, i + 1)
                for h in range(C):
                    cols = slice(h * P, (h + 1) * P)
                    ins = three_passes(ps_k[:, h, :],
                                       lambda c: w_hi["k"][:, c, cols], lambda c: w_lo["k"][:, c, cols],
                                       lambda c: xt_hi[:, par, c, :], lambda c: xt_lo[:, par, c, :])
                ins.then_inc(k_mm, 1)

            def project_v(i, par):
                for t in range(T):
                    toks = slice(t * P, (t + 1) * P)
                    ins = three_passes(ps_v[:, t, :],
                                       lambda c: xt_hi[:, par, c, toks], lambda c: xt_lo[:, par, c, toks],
                                       lambda c: w_hi["v"][:, c, :], lambda c: w_lo["v"][:, c, :])
                ins.then_inc(v_mm, 1)

            def project_q(i, par):
                for t in range(T):
                    toks = slice(t * P, (t + 1) * P)
                    three_passes(ps_q[:, t, :],
                                 lambda c: xt_hi[:, par, c, toks], lambda c: xt_lo[:, par, c, toks],
                                 lambda c: w_hi["q"][:, c, :], lambda c: w_lo["q"][:, c, :], last=False)
                    if isinstance(i, int) and i == 0 and t == 0:
                        pe.wait_ge(bq_rows_done, 3)
                    ins = mm(ps_q[:, t, :], bias_sel[:, :], bq_rows[:, :], start=False, stop=True)
                ins.then_inc(q_mm, 1)

            def transpose_ek(i):
                pe.wait_ge(ek_done, 2 * (i + 1))
                if not isinstance(i, int) or i >= 2:
                    pe.wait_ge(h_done, i - 1)
                for t in range(T):
                    for h in range(C):
                        ins = nc.tensor.transpose(ps_t[:, t, h * P:(h + 1) * P],
                                                  ek[:, h, t * P:(t + 1) * P], ident[:, :])
                ins.then_inc(ekt_mm, 1)

            def transpose_q(i):
                pe.wait_ge(q_sh_done, i + 1)
                for h in range(C):
                    for t in range(T):
                        ins = nc.tensor.transpose(ps_x[:, h, t * P:(t + 1) * P],
                                                  q_sh[:, t, h * P:(h + 1) * P], ident[:, :])
                ins.then_inc(qt_mm, 1)

            def context(i):
                pe.wait_ge(v_done, i + 1)
                pe.wait_ge(ek_tok_done, i + 1)
                if not isinstance(i, int) or i >= 1:
                    pe.wait_ge(ctx_m_done, 2 * i)
                for h in range(C):
                    cols = slice(h * P, (h + 1) * P)
                    for t in range(T):
                        ins = mm(ps_c[:, h, :], ek_tok[:, t, cols], v_tok[:, t, cols],
                                 start=(t == 0), stop=(t == T - 1))
                ins.then_inc(ctx_mm, 1)

            def attend(i):
                pe.wait_ge(eq_done, i + 1)
                pe.wait_ge(ctx_bd_done, i + 1)
                for t in range(T):
                    for h in range(C):
                        ins = mm(ps_y[:, t, h * HC * W:(h + 1) * HC * W], eq[:, h, t * P:(t + 1) * P],
                                 ctx_bd[:, h, :, :], start=True, stop=True)
                ins.then_inc(y_mm, 1)

            def transpose_y(i):
                pe.wait_ge(yhat_done, 2 * (i + 1))
                for h in range(C):
                    for t in range(T):
                        ins = nc.tensor.transpose(ps_t[:, h, t * P:(t + 1) * P],
                                                  yhat[:, t, h * P:(h + 1) * P], ident[:, :])
                ins.then_inc(yt_mm, 1)

            def step(i, par, last=False):
                project_k(i, par)
                transpose_q(i - 1)
                project_v(i, par)
                transpose_y(i - 2)
                if not last:
                    transpose_x(i + 1)
                attend(i - 1)
                transpose_ek(i)
                project_q(i, par)
                context(i)

            def project_out(b):
                pe.wait_ge(s_hi_done, b + 1)
                pe.wait_ge(s_lo_done, b + 1)
                if b >= 2:
                    pe.wait_ge(o_g_done, b - 1)
                for t in range(T):
                    toks = slice(t * P, (t + 1) * P)
                    ins = three_passes(ps_o[b % 2][:, t, :],
                                       lambda c: s_hi[:, b, c, toks], lambda c: s_lo[:, b, c, toks],
                                       lambda c: w_hi["o"][:, c, :], lambda c: w_lo["o"][:, c, :])
                ins.then_inc(o_mm, 1)

            pe.wait_ge(const_done, 2)
            keep_busy(12)
            pe.wait_ge(ident_done, 2)
            transpose_x(0)
            pe.wait_ge(vec_in, 16)
            pe.wait_ge(w_in["k"], 16)
            for h in range(C):
                for c in range(C):
                    ins = mm(ps_c[:, 1, h:h + 1], w_raw["k"][:, c, h * P:(h + 1) * P], b_v[:, c:c + 1],
                             start=(c == 0), stop=(c == C - 1))
            ins.then_inc(ck_mm_done, 1)
            pe.wait_ge(w_hi_done, 2)
            pe.wait_ge(w_lo_done, 2)
            project_k(0, 0)
            pe.wait_ge(w_hi_done, 4)
            pe.wait_ge(w_lo_done, 4)
            project_v(0, 0)
            transpose_x(1)
            pe.wait_ge(row_in, 16)
            pe.wait_ge(const_done, 2)
            for k, n in enumerate("qv"):
                pe.wait_ge(w_in[n], 16)
                for c in range(C):
                    mm(ps_y[:, 0, k * D:(k + 1) * D], b_v[:, c:c + 1].to_broadcast([P, P]),
                       w_raw[n][:, c, :], start=(c == 0), stop=False)
                mm(ps_y[:, 0, k * D:(k + 1) * D], ones[0:1, :], bqv_row[:, k, :],
                   start=False, stop=True).then_inc(cqv_mm_done, 1)
            transpose_ek(0)
            pe.wait_ge(w_hi_done, 6)
            pe.wait_ge(w_lo_done, 6)
            project_q(0, 0)
            pe.wait_ge(ck_done, 1)
            context(0)
            pe.wait_ge(silu_c_done, 1)
            pe.wait_ge(emb_in, 16)
            for j in range(2 * C):
                for c in range(C):
                    ins = mm(ps_y[:, 1, j * B:(j + 1) * B], emb_sb[:, c, j * P:(j + 1) * P],
                             silu_c[:, c, :], start=(c == 0), stop=(c == C - 1))
            ins.then_inc(emb_mm_done, 1)

            project_k(1, 1)
            transpose_q(0)
            project_v(1, 1)
            transpose_x(2)
            pe.wait_ge(affine_done, 2)
            attend(0)
            transpose_ek(1)
            project_q(1, 1)
            context(1)
            with pe.Fori(2, B - 3, 2) as i:
                step(i, 0)
                step(i + 1, 1)
            step(B - 2, 0)
            step(B - 1, 1, last=True)
            keep_busy(2)
            transpose_q(B - 1)
            keep_busy(3)
            attend(B - 1)
            keep_busy(4)
            pe.wait_ge(w_lo_done, 7)
            for b in range(B):
                project_out(b)
                if b == 0:
                    transpose_y(B - 2)
                if b == 2:
                    pe.wait_ge(h_done, B - 1)
                    transpose_y(B - 1)

        @block.vector
        def _(dve):
            def stats_x(i, t):
                dve.bn_stats(st1[:, t, :], x_all[:, i, t, :]).then_inc(st1_done, 1)

            def aggregate_x(i):
                dve.drain()
                for t in range(T):
                    dve.bn_aggr(mv1[:, t, :], st1[:, t, :]).then_inc(mv1_done, 1)

            def variance_x(i):
                dve.wait_ge(mv1_done, 2 * (i + 1))
                dve.tensor_scalar(ve1[:, :], mv1[:, :, 1], EPS, None, ALU.add).then_inc(ve1_done, 1)

            def mean_x(i):
                dve.wait_ge(rstd1_done, i + 1)
                if not isinstance(i, int) or i >= 1:
                    dve.wait_ge(xhat_done, i)
                dve.scalar_tensor_tensor(out=nmr1[:, :], in0=mv1[:, :, 0], scalar=-1.0, in1=rstd1[:, :],
                                         op0=ALU.mult, op1=ALU.mult).then_inc(nmr1_done, 1)

            def split_x(i, par):
                dve.wait_ge(xt_hi_done, i + 1)
                dve.tensor_tensor(xt_lo[:, par, :, :], ps_x[:, :, :], xt_hi[:, par, :, :].bitcast(F32),
                                  ALU.subtract).then_inc(xt_lo_done, 1)

            def k_max0(i):
                dve.wait_ge(k_mm, i + 1)
                dve.tensor_reduce(kmax0[:, :], ps_k[:, :, :], AX.X, ALU.max).then_inc(kmax0_done, 1)

            def k_max(i):
                dve.wait_ge(kmax0_done, i + 1)
                dve.tensor_tensor(kmax[:, :], kmax0[:, :], ck_sb[:, :], ALU.add).then_inc(kmax_done, 1)

            def k_bias(i):
                dve.wait_ge(kmax_done, i + 1)
                dve.tensor_tensor(kbias[:, :], ck_sb[:, :], kmax[:, :], ALU.subtract).then_inc(kbias_done, 1)

            def k_reciprocal(i):
                dve.wait_ge(ek_done, 2 * (i + 1))
                dve.reciprocal(krec[:, :], ksum[:, :]).then_inc(krec_done, 1)

            def q_max(i):
                dve.wait_ge(q_mm, i + 1)
                dve.tensor_reduce(qmax[:, :, :], ps_q[:, :, :].rearrange("p t (h d) -> p t h d", d=DH),
                                  AX.X, ALU.max).then_inc(qmax_done, 1)

            def q_shift(i):
                dve.wait_ge(qmax_done, i + 1)
                dve.tensor_tensor(q_sh[:, :, :].rearrange("p t (h d) -> p (t h) d", d=DH),
                                  ps_q[:, :, :].rearrange("p t (h d) -> p (t h) d", d=DH),
                                  qmax[:, :, :].rearrange("p t h -> p (t h)").unsqueeze(2)
                                  .to_broadcast([P, T * HEADS, DH]),
                                  ALU.subtract).then_inc(q_sh_done, 1)

            def mask_context(i):
                dve.wait_ge(ctx_mm, i + 1)
                dve.wait_ge(krec_done, i + 1)
                for h in range(C):
                    dve.scalar_tensor_tensor(out=ctx_m[:, h, :, :],
                                             in0=ps_c[:, h, :].rearrange("p (j d) -> p j d", d=DH),
                                             scalar=krec[:, h:h + 1], in1=head_mask[:, :, 0:DH],
                                             op0=ALU.mult, op1=ALU.mult).then_inc(ctx_m_done, 1)

            def scale_y(i):
                dve.wait_ge(y_mm, i + 1)
                heads = ps_y[:, :, 0:HEADS * W].rearrange("p t (h w) -> p t h w", w=W)
                dve.reciprocal(qrec[:, :, :], heads[:, :, :, DH]).then_inc(qrec_done, 1)
                dve.wait_ge(qrec_done, i + 1)
                dve.tensor_tensor(y[:, :, :].rearrange("p t (h d) -> p t h d", d=DH), heads[:, :, :, 0:DH],
                                  qrec[:, :, :].unsqueeze(3).to_broadcast([P, T, HEADS, DH]),
                                  ALU.mult).then_inc(y_done, 1)

            def stats_y(i):
                dve.wait_ge(y_done, i + 1)
                for t in range(T):
                    dve.bn_stats(st2[:, t, :], y[:, t, :]).then_inc(st2_done, 1)

            def aggregate_y(i):
                dve.drain()
                for t in range(T):
                    dve.bn_aggr(mv2[:, t, :], st2[:, t, :]).then_inc(mv2_done, 1)

            def variance_y(i):
                dve.wait_ge(mv2_done, 2 * (i + 1))
                dve.tensor_scalar(ve2[:, :], mv2[:, :, 1], EPS, None, ALU.add).then_inc(ve2_done, 1)

            def normalise_y(i, t):
                dve.wait_ge(rstd2_done, i + 1)
                dve.tensor_scalar(yhat[:, t, :], y[:, t, :], mv2[:, t, 0:1], rstd2[:, t:t + 1],
                                  ALU.subtract, ALU.mult).then_inc(yhat_done, 1)

            def step(i, par, last=False, stats=True):
                if not last:
                    mean_x(i + 1)
                q_max(i - 1)
                aggregate_y(i - 2)
                q_shift(i - 1)
                variance_y(i - 2)
                mask_context(i - 1)
                k_max0(i)
                normalise_y(i - 2, 0)
                k_max(i)
                normalise_y(i - 2, 1)
                k_bias(i)
                if stats:
                    stats_x(i + 2, 0)
                    stats_x(i + 2, 1)
                    aggregate_x(i + 2)
                    variance_x(i + 2)
                scale_y(i - 1)
                if not last:
                    split_x(i + 1, 1 - par)
                k_reciprocal(i)
                stats_y(i - 1)

            def split_s(b):
                dve.wait_ge(s_f_done, b + 1)
                dve.wait_ge(s_hi_done, b + 1)
                dve.tensor_tensor(s_lo[:, b, :, :], s_f[:, b, :, :], s_hi[:, b, :, :].bitcast(F32),
                                  ALU.subtract).then_inc(s_lo_done, 1)

            def gate_o(b):
                dve.wait_ge(o_mm, b + 1)
                if b >= 2:
                    dve.wait_ge(res_done, b - 1)
                dve.tensor_tensor(o_g[:, b % 2, :, :], ps_o[b % 2][:, :, :],
                                  gate_bc[:, b, :].unsqueeze(1).to_broadcast([P, T, D]),
                                  ALU.mult).then_inc(o_g_done, 1)

            def weight_lo(n, k):
                for c in range(C):
                    dve.wait_ge(w_hi_done, 2 * k + c + 1)
                    dve.scalar_tensor_tensor(out=w_lo[n][:, c, :], in0=w_raw[n][:, c, :], scalar=g_v[:, c:c + 1],
                                             in1=w_hi[n][:, c, :].bitcast(F32), op0=ALU.mult,
                                             op1=ALU.subtract).then_inc(w_lo_done, 1)

            def all_stats(i):
                dve.wait_ge(x_in[min(i, 2)], 16)
                for t in range(T):
                    stats_x(i, t)
                aggregate_x(i)
                variance_x(i)

            all_stats(0)
            mean_x(0)
            dve.wait_ge(vec_in, 16)
            weight_lo("k", 0)
            dve.wait_ge(silu_e_done, 1)
            dve.tensor_scalar(silu_1e[:, :, :], silu_e[:, :, :], 1.0, None, ALU.add).then_inc(small_done, 1)
            dve.wait_ge(small_done, 1)
            dve.reciprocal(silu_r[:, :, :], silu_1e[:, :, :]).then_inc(small_done, 1)
            all_stats(1)
            split_x(0, 0)
            dve.wait_ge(small_done, 2)
            dve.tensor_tensor(silu_c[:, :, :], silu_r[:, :, :], cond_v, ALU.mult).then_inc(silu_c_done, 1)
            mean_x(1)
            weight_lo("v", 1)
            dve.wait_ge(ck_mm_done, 1)
            dve.tensor_tensor(ck_sb[:, :], ps_c[:, 1, 0:C], bk_v, ALU.add).then_inc(ck_done, 1)
            dve.wait_ge(ck_done, 1)
            k_max0(0)
            k_max(0)
            k_bias(0)
            weight_lo("q", 2)
            split_x(1, 1)
            dve.wait_ge(cqv_mm_done, 2)
            dve.tensor_copy(bq_rows[0:64, :], ps_y[0:64, 0, 0:D]).then_inc(bq_rows_done, 1)
            dve.tensor_copy(bq_hi[64:P, :], ps_y[64:P, 0, 0:D]).then_inc(small_done, 1)
            dve.wait_ge(small_done, 3)
            dve.tensor_tensor(bq_rows[64:P, :], ps_y[64:P, 0, 0:D], bq_hi[64:P, :].bitcast(F32),
                              ALU.subtract).then_inc(bq_rows_done, 1)
            k_reciprocal(0)
            all_stats(2)
            dve.wait_ge(mask_done, 3)
            for h in range(C):
                ins = dve.tensor_tensor(cv_blk[:, h, :, :],
                                        ps_y[:, 0, D + h * P:D + (h + 1) * P].rearrange("p (j d) -> p j d", d=DH),
                                        head_mask[:, :, 0:DH], ALU.mult)
            ins.then_inc(cv_done, 1)

            q_max(0)
            mean_x(2)
            q_shift(0)
            mask_context(0)
            k_max0(1)
            dve.wait_ge(emb_mm_done, 1)
            dve.tensor_tensor(emb_o[:, :, :], ps_y[:, 1, 0:2 * C * B].rearrange("p (j b) -> p j b", b=B),
                              embb_v.unsqueeze(2).to_broadcast([P, 2 * C, B]), ALU.add).then_inc(small_done, 1)
            k_max(1)
            dve.wait_ge(small_done, 4)
            dve.tensor_scalar(scale1[:, :, :], emb_o[:, 0:C, :], 1.0, None, ALU.add).then_inc(small_done, 1)
            k_bias(1)
            dve.wait_ge(small_done, 5)
            dve.tensor_tensor(h_scale[:, :, :].rearrange("p b c -> p c b"), scale1[:, :, :],
                              sng_v.unsqueeze(2).to_broadcast([P, C, B]), ALU.mult).then_inc(affine_done, 1)
            dve.tensor_tensor(shift_t[:, :, :], scale1[:, :, :],
                              snb_v.unsqueeze(2).to_broadcast([P, C, B]), ALU.mult).then_inc(small_done, 1)
            stats_x(3, 0)
            dve.wait_ge(small_done, 6)
            dve.tensor_tensor(h_bias[:, :, :].rearrange("p b c -> p c b"), shift_t[:, :, :],
                              emb_o[:, C:2 * C, :], ALU.add).then_inc(affine_done, 1)
            stats_x(3, 1)
            aggregate_x(3)
            split_x(2, 0)
            variance_x(3)
            k_reciprocal(1)
            scale_y(0)
            stats_y(0)

            with dve.Fori(2, B - 3, 2) as i:
                step(i, 0)
                step(i + 1, 1)
            step(B - 2, 0, stats=False)
            step(B - 1, 1, last=True, stats=False)
            q_max(B - 1)
            aggregate_y(B - 2)
            q_shift(B - 1)
            variance_y(B - 2)
            mask_context(B - 1)
            normalise_y(B - 2, 0)
            normalise_y(B - 2, 1)
            split_s(0)
            scale_y(B - 1)
            split_s(1)
            stats_y(B - 1)
            aggregate_y(B - 1)
            variance_y(B - 1)
            dve.wait_ge(gate_in, 32)
            gate_o(0)
            split_s(2)
            gate_o(1)
            dve.wait_ge(yt_mm, B - 1)
            normalise_y(B - 1, 0)
            normalise_y(B - 1, 1)
            split_s(3)
            split_s(4)
            for b in range(2, B):
                gate_o(b)
                if b + 3 < B:
                    split_s(b + 3)

        @block.scalar
        def _(act):
            def normalise_x(i):
                act.wait_ge(nmr1_done, i + 1)
                if not isinstance(i, int) or i >= 1:
                    act.wait_ge(xt_mm, i)
                for t in range(T):
                    ins = nc.scalar.activation(xhat[:, t, :], x_all[:, i, t, :], ACT.Identity,
                                               scale=rstd1[:, t:t + 1], bias=nmr1[:, t:t + 1])
                ins.then_inc(xhat_done, 1)

            def hi_x(i, par):
                act.wait_ge(xt_mm, i + 1)
                if not isinstance(i, int) or i >= 2:
                    act.wait_ge(q_mm, i - 1)
                nc.scalar.activation(xt_hi[:, par, :, :], ps_x[:, :, :], ACT.Identity).then_inc(xt_hi_done, 1)

            def exp_k(i):
                act.wait_ge(kbias_done, i + 1)
                if not isinstance(i, int) or i >= 1:
                    act.wait_ge(ekt_mm, i)
                    act.wait_ge(krec_done, i)
                for h in range(C):
                    nc.scalar.activation(ek[:, h, :], ps_k[:, h, :], ACT.Exp, bias=kbias[:, h:h + 1],
                                         accum_out=ksum[:, h:h + 1]).then_inc(ek_done, 1)

            def copy_v(i):
                act.wait_ge(v_mm, i + 1)
                if not isinstance(i, int) or i >= 1:
                    act.wait_ge(ctx_mm, i)
                nc.scalar.activation(v_tok[:, :, :], ps_v[:, :, :], ACT.Identity).then_inc(v_done, 1)

            def copy_ek(i):
                act.wait_ge(ekt_mm, i + 1)
                nc.scalar.activation(ek_tok[:, :, :], ps_t[:, :, :], ACT.Identity).then_inc(ek_tok_done, 1)

            def exp_q(i):
                act.wait_ge(qt_mm, i + 1)
                if not isinstance(i, int) or i >= 1:
                    act.wait_ge(y_mm, i)
                nc.scalar.activation(eq[:, :, :], ps_x[:, :, :], ACT.Exp).then_inc(eq_done, 1)

            def affine_y(i):
                act.wait_ge(yt_mm, i + 1)
                for h in range(C):
                    ins = nc.scalar.activation(h_all[:, i, h, :], ps_t[:, h, :], ACT.Identity,
                                               scale=h_scale[:, i, h:h + 1], bias=h_bias[:, i, h:h + 1])
                ins.then_inc(h_done, 1)

            def step(i, par, second=False, last=False):
                if not last:
                    normalise_x(i + 1)
                exp_q(i - 1)
                exp_k(i)
                if not second:
                    affine_y(i - 2)
                copy_v(i)
                if not last:
                    hi_x(i + 1, 1 - par)
                copy_ek(i)

            def silu(b):
                nc.scalar.activation(s_f[:, b, :, :], h_all[:, b, :, :], ACT.Silu).then_inc(s_f_done, 1)
                nc.scalar.activation(s_hi[:, b, :, :], h_all[:, b, :, :], ACT.Silu).then_inc(s_hi_done, 1)

            def weight_hi(n):
                act.wait_ge(w_in[n], 16)
                for c in range(C):
                    nc.scalar.activation(w_hi[n][:, c, :], w_raw[n][:, c, :], ACT.Identity,
                                         scale=g_v[:, c:c + 1]).then_inc(w_hi_done, 1)

            act.dma_start(vec[:, :], vectors).then_inc(vec_in, 16)
            act.dma_start(bqv_row[:, :, :], bqv).then_inc(row_in, 16)
            act.wait_ge(vec_in, 16)
            nc.scalar.activation(silu_e[:, :, :], cond_v, ACT.Exp, scale=-1.0).then_inc(silu_e_done, 1)
            weight_hi("k")
            normalise_x(0)
            hi_x(0, 0)
            weight_hi("v")
            normalise_x(1)
            exp_k(0)
            weight_hi("q")
            hi_x(1, 1)
            copy_v(0)
            copy_ek(0)
            act.wait_ge(w_in["o"], 16)
            nc.scalar.activation(w_hi["o"][:, :, :], w_raw["o"][:, :, :], ACT.Identity).then_inc(w_hi_done, 1)
            step(1, 1, second=True)
            act.wait_ge(affine_done, 2)
            with act.Fori(2, B - 3, 2) as i:
                step(i, 0)
                step(i + 1, 1)
            step(B - 2, 0)
            step(B - 1, 1, last=True)
            exp_q(B - 1)
            act.wait_ge(h_done, B - 2)
            silu(0)
            silu(1)
            silu(2)
            affine_y(B - 2)
            silu(3)
            silu(4)
            silu(5)
            affine_y(B - 1)
            act.wait_ge(h_done, B)
            with act.Fori(6, B) as b:
                silu(b)

        @block.gpsimd
        def _(pool):
            def power(rstd, ve):
                return nc.gpsimd.tensor_tensor(rstd[:, :], ve[:, :], minus_half[:, :], ALU.pow)

            def rstd_x(i):
                pool.wait_ge(ve1_done, i + 1)
                if not isinstance(i, int) or i >= 1:
                    pool.wait_ge(xhat_done, i)
                power(rstd1, ve1).then_inc(rstd1_done, 1)

            def rstd_y(i):
                pool.wait_ge(ve2_done, i + 1)
                power(rstd2, ve2).then_inc(rstd2_done, 1)

            def finish_context(i):
                pool.wait_ge(ctx_m_done, 2 * (i + 1))
                for h in range(C):
                    ins = nc.gpsimd.tensor_tensor(ctx_bd[:, h, :, 0:DH], ctx_m[:, h, :, :],
                                                  cv_blk[:, h, :, :], ALU.add)
                ins.then_inc(ctx_bd_done, 1)

            def residual(i):
                pool.wait_ge(xhat_done, i + 1)
                if not isinstance(i, int) or i >= 1:
                    pool.wait_ge(xres_done, i)
                nc.gpsimd.tensor_tensor(gob[:, :], gate_bc[:, i, :], outb_bc[:, :], ALU.mult).then_inc(gob_done, 1)
                pool.wait_ge(gob_done, i + 1)
                nc.gpsimd.tensor_tensor(x_all[:, i, :, :], x_all[:, i, :, :],
                                        gob[:, :].unsqueeze(1).to_broadcast([P, T, D]),
                                        ALU.add).then_inc(xres_done, 1)

            def step(i, stats=True):
                rstd_y(i - 2)
                finish_context(i - 1)
                if stats:
                    rstd_x(i + 2)
                residual(i - 1)

            def add_residual(b, par):
                pool.wait_ge(o_g_done, b + 1)
                nc.gpsimd.tensor_tensor(x_all[:, b, :, :], o_g[:, par, :, :], x_all[:, b, :, :],
                                        ALU.add).then_inc(res_done, 1)

            nc.gpsimd.memset(ones[:, :], 1.0).then_inc(const_done, 1)
            nc.gpsimd.memset(minus_half[:, :], -0.5).then_inc(const_done, 1)
            nc.gpsimd.memset(ident[:, :], 0.0).then_inc(ident_done, 1)
            pool.wait_ge(ident_done, 1)
            nc.gpsimd.affine_select(out=ident[:, :], in_=ident[:, :], compare_op=ALU.not_equal, fill=1.0, base=0,
                                    pattern=[[-1, P]], channel_multiplier=1).then_inc(ident_done, 1)
            pool.wait_ge(const_done, 2)
            nc.gpsimd.affine_select(out=bias_row0[:, :], in_=ones[:, :], compare_op=ALU.is_equal, fill=0.0, base=0,
                                    pattern=[[0, P]], channel_multiplier=1).then_inc(row0_done, 1)
            pool.wait_ge(row0_done, 1)
            nc.gpsimd.affine_select(out=bias_sel[:, :], in_=bias_row0[:, :], compare_op=ALU.not_equal, fill=1.0,
                                    base=-64, pattern=[[0, P]], channel_multiplier=1).then_inc(bq_rows_done, 1)
            nc.gpsimd.memset(head_mask[:, :, :], 1.0).then_inc(mask_done, 1)
            pool.wait_ge(mask_done, 1)
            for n, (sign, base) in enumerate(((1, 0), (-1, DH - 1))):
                nc.gpsimd.affine_select(out=head_mask[:, :, :], in_=head_mask[:, :, :], compare_op=ALU.is_ge,
                                        fill=0.0, base=base, pattern=[[-sign * DH, HC], [0, W]],
                                        channel_multiplier=sign).then_inc(mask_done, 1)
                pool.wait_ge(mask_done, n + 2)
            rstd_x(0)
            for h in range(C):
                nc.gpsimd.tensor_copy(ctx_bd[:, h, :, DH:W], head_mask[:, :, DH:W]).then_inc(const_done, 1)
            pool.wait_ge(const_done, 4)
            rstd_x(1)
            rstd_x(2)
            pool.wait_ge(w_hi_done, 7)
            nc.gpsimd.tensor_tensor(w_lo["o"][:, :, :], w_raw["o"][:, :, :], w_hi["o"][:, :, :].bitcast(F32),
                                    ALU.subtract).then_inc(w_lo_done, 1)
            pool.wait_ge(cv_done, 1)
            finish_context(0)
            rstd_x(3)
            pool.wait_ge(gate_in, 32)
            residual(0)
            with pool.Fori(2, B - 2) as i:
                step(i)
            step(B - 2, stats=False)
            step(B - 1, stats=False)
            rstd_y(B - 2)
            finish_context(B - 1)
            residual(B - 1)
            rstd_y(B - 1)
            pool.wait_ge(xres_done, B)
            with pool.Fori(0, B - 1, 2) as b:
                add_residual(b, 0)
                add_residual(b + 1, 1)


def kernel(**inputs):
    import concourse.bacc as bacc
    from concourse.bass_utils import run_bass_kernel_spmd

    a = {n.removeprefix("L0_cond_"): np.ascontiguousarray(v) for n, v in inputs.items()}
    vectors = [a[n].reshape(-1, P) for n in ("cond_1024", "norm_g", "norm_b", "bk", "sn_g", "sn_b", "emb_b")]
    a["vectors"] = np.ascontiguousarray(np.concatenate(vectors).T)
    a["bqv"] = np.stack([a["bq"], a["bv"]])[None]

    nc = bacc.Bacc("TRN2", target_bir_lowering=False, num_devices=1)
    arrays, args = {}, []
    for name in ("x", "cond_1024", "Wq", "Wk", "Wv", "emb_W", "out_W", "out_b", "vectors", "bqv"):
        arrays[f"in_{name}"] = a[name]
        args.append(nc.dram_tensor(f"in_{name}", a[name].shape, mybir.dt.from_np(a[name].dtype),
                                   kind="ExternalInput").ap())
    args.append(nc.dram_tensor("out_0", a["x"].shape, F32, kind="ExternalOutput").ap())
    linear_attention_block(nc, *args)
    r = run_bass_kernel_spmd(nc, [arrays], core_ids=[0])
    return r.results[0]["out_0"]
```
